# Optimizing a Trainium2 kernel written in Bass

```python
import numpy as np
import jax
import jax.numpy as jnp

def _softmax(x, axis=-1):
    return jax.nn.softmax(x, axis=axis)

def _gelu(x):
    return jax.nn.gelu(x, approximate=True)

def _silu(x):
    return jax.nn.silu(x)

def _sigmoid(x):
    return jax.nn.sigmoid(x)

def _layernorm(x, axis=-1, eps=1e-05):
    m = jnp.mean(x, axis=axis, keepdims=True)
    v = jnp.var(x, axis=axis, keepdims=True)
    return (x - m) / jnp.sqrt(v + eps)

def _scatter_add(tgt, idx, src, axis=0):
    return tgt.at[idx].add(src)

def _segment_sum(src, seg, n):
    return jax.ops.segment_sum(src, seg, n)
kernel_name = 'mk_rec_standalone_d1_rec_r8_6fee3a'

def setup_inputs(seed: int=0):
    np.random.seed(seed)
    _w = jnp.asarray

    def _rec_inputs():
        import jax
        import jax.numpy as jnp
        _rk = jax.random.key(seed)
        r_x = jax.random.randint(jax.random.fold_in(_rk, 1), (2048, 1024), 0, 2, jnp.int32)
        return r_x
    r_x = _rec_inputs()

    def _L0_rec_setup():
        import jax, jax.numpy as jnp
        import numpy as np
        BATCH = 2048
        NUM_CATEGORIES = 1024
        EMBED_DIM = 512
        key = jax.random.key(seed)
        kx, kw = jax.random.split(key)
        x = jax.random.randint(kx, (BATCH, NUM_CATEGORIES), 0, 2, dtype=jnp.int32)
        W = jax.random.normal(kw, (NUM_CATEGORIES, EMBED_DIM), dtype=jnp.float32)
        return {'x': x, 'W': W}
    _L0_rec_all = _L0_rec_setup()
    _L0_rec_in = {k: v for k, v in _L0_rec_all.items() if k in ('W',)}
    del _L0_rec_all
    return {'r_x': r_x, 'L0_rec_W': _L0_rec_in['W']}

def reference(r_x, L0_rec_W):
    import jax
    import jax.numpy as jnp

    def _L0_rec_ref(x, W):
        import jax, jax.numpy as jnp
        import numpy as np
        BATCH = 2048
        NUM_CATEGORIES = 1024
        EMBED_DIM = 512
        mask = (x != 0).astype(W.dtype)
        return jnp.einsum('bv,vd->bd', mask, W)
    y = _L0_rec_ref(r_x, L0_rec_W)
    return y

_drawn_inputs = setup_inputs


def setup_inputs(seed=0):
    import zlib

    import numpy as np

    out = dict(_drawn_inputs(seed))
    spreads = {}
    factors = {}
    for name, (base, spread) in spreads.items():
        noise = np.random.default_rng([zlib.crc32(name.encode()), seed]).standard_normal(out[name].shape)
        drawn = base * np.exp(spread * noise) if base else spread * noise
        out[name] = jnp.asarray(drawn.astype(out[name].dtype))
    for name, factor in factors.items():
        out[name] = (out[name] * factor).astype(out[name].dtype)
    return out
```

```python
from contextlib import ExitStack

import concourse.bass as bass
from concourse import mybir

P = 128
Q = 32
QUADS = P // Q
SLOTS = 4
HALVES = 2
WARM_MATMULS = 14

ALU = mybir.AluOpType
F32 = mybir.dt.float32
F32R = mybir.dt.float32r
I32 = mybir.dt.int32
BF16 = mybir.dt.bfloat16
DMA = 16


def masked_sum_kernel(nc: bass.Bass, r_x: bass.AP, w: bass.AP, out: bass.AP):
    B, V = r_x.shape
    D = w.shape[1]
    CHUNKS = V // P
    HC = CHUNKS // HALVES
    TILES = B // P
    GROUPS = TILES // SLOTS
    assert V % P == 0 and B % (P * SLOTS) == 0 and D * 4 <= 2048 and HC == SLOTS

    x_dram = r_x.rearrange("(t g q) (i v) -> t i q g v", g=QUADS, q=Q, i=QUADS)
    w_dram = w.rearrange("(i c w) d -> i c w d", i=QUADS, w=Q)
    out_dram = out.rearrange("(t p) d -> t p d", p=P)

    with ExitStack() as ctx:
        def sb(name, shape, dt):
            return ctx.enter_context(nc.sbuf_tensor(name, shape, dt))

        def sem(name):
            return ctx.enter_context(nc.semaphore(name))

        w_raw = sb("w_raw", [P, CHUNKS, D], F32)
        w_hi = sb("w_hi", [P, CHUNKS, D], F32R)
        w_lo = sb("w_lo", [P, CHUNKS, D], F32R)
        raw = sb("raw", [P, SLOTS, QUADS, CHUNKS, Q], I32)
        turned = sb("turned", [P, 2, CHUNKS * P], I32)
        first_mask = sb("first_mask", [P, SLOTS, CHUNKS, P], F32R)
        mask = sb("mask", [P, SLOTS, CHUNKS, P], F32R)
        out_sb = sb("out_sb", [P, SLOTS, D], F32)
        warm = sb("warm", [P, D], BF16)
        first_acc = [ctx.enter_context(nc.psum_tensor(f"first_acc{s}", [P, D], F32)) for s in range(SLOTS)]
        acc = [ctx.enter_context(nc.psum_tensor(f"acc{s}", [P, D], F32)) for s in range(SLOTS)]

        first_x_landed = [[sem(f"first_x_landed_{h}_{s}") for s in range(SLOTS)] for h in range(HALVES)]
        x_landed = [sem(f"x_landed{s}") for s in range(SLOTS)]
        w_landed = [sem(f"w_landed{c}") for c in range(CHUNKS)]
        out_stored = [sem(f"out_stored{s}") for s in range(SLOTS)]
        warm_ready = sem("warm_ready")
        hi_ready = sem("hi_ready")
        lo_ready = sem("lo_ready")
        turned_done = sem("turned_done")
        mask_ready = sem("mask_ready")
        product_done = sem("product_done")
        copied = sem("copied")

        FIRST_STEPS = HALVES * SLOTS
        LOAD = QUADS * DMA

        block = ctx.enter_context(nc.Block())

        def load_first(eng, quads, h, s):
            for i in quads:
                eng.dma_start(raw[Q * i:Q * (i + 1), s, :, HC * h:HC * (h + 1), :],
                              x_dram[s, i, :, :, HC * Q * h:HC * Q * (h + 1)].rearrange("q g (c w) -> q g c w", w=Q)
                              ).then_inc(first_x_landed[h][s], DMA)

        def load_w(eng, quads, c):
            for i in quads:
                eng.dma_start(w_raw[Q * i:Q * (i + 1), c, :], w_dram[i, c]).then_inc(w_landed[c], DMA)

        def load_first_group(eng, quads):
            for h in range(HALVES):
                for n in range(SLOTS):
                    load_first(eng, quads, h, n)
                    load_w(eng, quads, HC * h + n)

        @block.sync
        def _(sp):
            load_first_group(sp, (0, 1))
            with sp.Fori(1, GROUPS) as k:
                for s in range(SLOTS):
                    if s == 0:
                        pass
                    sp.wait_ge(turned_done, FIRST_STEPS + SLOTS * (k - 2) + s + 1)
                    for i in (0, 2, 1, 3):
                        sp.dma_start(raw[Q * i:Q * (i + 1), s, :, :, :],
                                     x_dram[SLOTS * k + s, i]).then_inc(x_landed[s], DMA)

        @block.scalar
        def _(act):
            load_first_group(act, (2, 3))
            for c in range(CHUNKS):
                act.wait_ge(w_landed[c], LOAD)
                nc.scalar.copy(w_hi[:, c, :], w_raw[:, c, :]).then_inc(hi_ready, 1)
            for s in range(SLOTS):
                act.wait_ge(product_done, s + 1)
                nc.scalar.copy(out_sb[:, s, :], first_acc[s][:, :]).then_inc(copied, 1)
                act.wait_ge(copied, s + 1)
                act.dma_start(out_dram[s], out_sb[:, s, :]).then_inc(out_stored[s], DMA)
            with act.Fori(1, GROUPS) as k:
                for s in range(SLOTS):
                    act.wait_ge(product_done, SLOTS * k + s + 1)
                    act.wait_ge(out_stored[s], DMA * k)
                    nc.scalar.copy(out_sb[:, s, :], acc[s][:, :]).then_inc(copied, 1)
                    act.wait_ge(copied, SLOTS * k + s + 1)
                    act.dma_start(out_dram[SLOTS * k + s], out_sb[:, s, :]).then_inc(out_stored[s], DMA)
            for s in range(SLOTS):
                act.wait_ge(out_stored[s], DMA * GROUPS)

        @block.vector
        def _(dve):
            nc.vector.memset(warm[:, :], 0.0).then_inc(warm_ready, 1)

            def low_part(c):
                dve.wait_ge(hi_ready, c + 1)
                nc.vector.tensor_tensor(w_lo[:, c, :], w_raw[:, c, :], w_hi[:, c, :].bitcast(F32),
                                        ALU.subtract).then_inc(lo_ready, 1)

            step = 0
            for h in range(HALVES):
                for n in range(SLOTS):
                    chunks = slice(HC * h, HC * (h + 1))
                    dve.wait_ge(first_x_landed[h][n], LOAD)
                    nc.vector.transpose(
                        turned[:, step % 2, 0:HC * P].rearrange("p (c g q) -> p c g q", c=HC, g=QUADS),
                        raw[:, n, :, chunks, :].rearrange("p g c w -> p c g w")).then_inc(turned_done, 1)
                    dve.wait_ge(turned_done, step + 1)
                    nc.vector.tensor_scalar(first_mask[:, n, chunks, :],
                                            turned[:, step % 2, 0:HC * P].rearrange("p (c b) -> p c b", c=HC),
                                            0.0, None, ALU.not_equal).then_inc(mask_ready, 1)
                    low_part(HC * h + n)
                    step += 1
            with dve.Fori(1, GROUPS) as k:
                for s in range(SLOTS):
                    dve.wait_ge(x_landed[s], LOAD * k)
                    nc.vector.transpose(
                        turned[:, s % 2, :].rearrange("p (c g q) -> p c g q", c=CHUNKS, g=QUADS),
                        raw[:, s, :, :, :].rearrange("p g c w -> p c g w")).then_inc(turned_done, 1)
                    dve.wait_ge(turned_done, FIRST_STEPS + SLOTS * (k - 1) + s + 1)
                    dve.wait_ge(product_done, SLOTS * (k - 1) + s + 1)
                    nc.vector.tensor_scalar(mask[:, s, :, :],
                                            turned[:, s % 2, :].rearrange("p (c b) -> p c b", c=CHUNKS),
                                            0.0, None, ALU.not_equal).then_inc(mask_ready, 1)

        @block.tensor
        def _(pe):
            pe.wait_ge(warm_ready, 1)
            for n in range(WARM_MATMULS):
                nc.tensor.matmul(acc[0][:, :], warm[:, 0:P], warm[:, :], start=True, stop=True)

            def unit(s, c):
                nc.tensor.matmul(first_acc[s][:, :], first_mask[:, s, c, :], w_hi[:, c, :],
                                 start=(c == 0), stop=False)
                return nc.tensor.matmul(first_acc[s][:, :], first_mask[:, s, c, :], w_lo[:, c, :],
                                        start=False, stop=(c == CHUNKS - 1))

            for h in range(HALVES):
                for n in range(SLOTS):
                    pe.wait_ge(mask_ready, SLOTS * h + n + 1)
                    for c in range(HC * h, HC * h + n):
                        unit(n, c)
                    pe.wait_ge(lo_ready, HC * h + n + 1)
                    for s in range(n + 1):
                        last = unit(s, HC * h + n)
                        if HC * h + n == CHUNKS - 1:
                            last.then_inc(product_done, 1)
            with pe.Fori(1, GROUPS) as k:
                for s in range(SLOTS):
                    pe.wait_ge(mask_ready, FIRST_STEPS + SLOTS * (k - 1) + s + 1)
                    pe.wait_ge(copied, SLOTS * (k - 1) + s + 1)
                    for c in range(CHUNKS):
                        nc.tensor.matmul(acc[s][:, :], mask[:, s, c, :], w_hi[:, c, :],
                                         start=(c == 0), stop=False)
                        last = nc.tensor.matmul(acc[s][:, :], mask[:, s, c, :], w_lo[:, c, :],
                                                start=False, stop=(c == CHUNKS - 1))
                    last.then_inc(product_done, 1)


def kernel(r_x, L0_rec_W):
    import numpy as np
    import concourse.bacc as bacc
    from concourse.bass_utils import run_bass_kernel_spmd

    nc = bacc.Bacc("TRN2", target_bir_lowering=False, num_devices=1)
    arrays = {"r_x": np.ascontiguousarray(r_x), "w": np.ascontiguousarray(L0_rec_W)}
    aps = [nc.dram_tensor(name, a.shape, mybir.dt.from_np(a.dtype), kind="ExternalInput").ap()
           for name, a in arrays.items()]
    out = nc.dram_tensor("out", (r_x.shape[0], L0_rec_W.shape[1]), F32, kind="ExternalOutput").ap()
    masked_sum_kernel(nc, *aps, out)
    return run_bass_kernel_spmd(nc, [arrays], core_ids=[0]).results[0]["out"]
```

```python
from contextlib import ExitStack

import concourse.bass as bass
from concourse import mybir

P = 128
Q = 32
QUADS = P // Q
SLOTS = 4
PAIR = 2
WARM_MATMULS = 12

ALU = mybir.AluOpType
F32 = mybir.dt.float32
F32R = mybir.dt.float32r
I32 = mybir.dt.int32
U32 = mybir.dt.uint32
U8 = mybir.dt.uint8
BF16 = mybir.dt.bfloat16
DMA = 16
WORD = 4


def masked_sum_kernel(nc: bass.Bass, r_x: bass.AP, w: bass.AP, out: bass.AP):
    B, V = r_x.shape
    D = w.shape[1]
    CHUNKS = V // P
    WORDS = CHUNKS // WORD
    TILES = B // P
    GROUPS = TILES // SLOTS
    assert V % (P * WORD) == 0 and B % (P * SLOTS) == 0 and D * 4 <= 2048

    x_dram = r_x.rearrange("(tg q) (i v) -> i q tg v", q=Q, i=QUADS)
    w_dram = w.rearrange("(p c) d -> p c d", p=P)
    out_dram = out.rearrange("(t p) d -> t p d", p=P)

    with ExitStack() as ctx:
        def sb(name, shape, dt):
            return ctx.enter_context(nc.sbuf_tensor(name, shape, dt))

        def sem(name):
            return ctx.enter_context(nc.semaphore(name))

        w_raw = sb("w_raw", [P, CHUNKS, D], F32)
        w_hi = sb("w_hi", [P, CHUNKS, D], F32R)
        w_lo = sb("w_lo", [P, CHUNKS, D], F32R)
        raw = sb("raw", [P, SLOTS, QUADS * CHUNKS * Q], I32)
        small = sb("small", [P, 2, QUADS * Q * CHUNKS], U8)
        turned = sb("turned", [P, SLOTS, WORDS * P * WORD], U8)
        first_mask = sb("first_mask", [P, SLOTS, CHUNKS, P], F32R)
        mask = sb("mask", [P, SLOTS, CHUNKS, P], F32R)
        out_sb = sb("out_sb", [P, SLOTS, D], F32)
        warm = sb("warm", [P, D], BF16)
        acc = [ctx.enter_context(nc.psum_tensor(f"acc{s}", [P, D], F32)) for s in range(SLOTS)]
        warm_acc = ctx.enter_context(nc.psum_tensor("warm_acc", [P, D], F32))

        first_x_landed = [sem(f"first_x_landed{s}") for s in range(SLOTS)]
        x_landed = [sem(f"x_landed{j}") for j in range(SLOTS // PAIR)]
        w_landed = [sem(f"w_landed{c}") for c in range(CHUNKS)]
        out_stored = [sem(f"out_stored{s}") for s in range(SLOTS)]
        warm_ready = sem("warm_ready")
        hi_ready = sem("hi_ready")
        lo_ready = sem("lo_ready")
        small_ready = sem("small_ready")
        turned_ready = sem("turned_ready")
        mask_ready = sem("mask_ready")
        product_done = sem("product_done")
        copied = sem("copied")
        LOAD = QUADS * DMA

        ORDER = "x0 w0 w1 w2 x1 w3 w4 x2 w5 w6 x3 w7".split()
        SCALAR_ORDER = "w0 w1 x0 w2 w3 x1 w4 x2 w5 w6 x3 w7".split()
        FIRST_MASKS = SLOTS * WORDS

        block = ctx.enter_context(nc.Block())

        def store(eng, tile, s):
            eng.wait_ge(copied, tile + 1)
            eng.dma_start(out_dram[tile], out_sb[:, s, :]).then_inc(out_stored[s], DMA)

        @block.sync
        def _(sp):
            for s in range(SLOTS):
                for i in (0, 2, 1, 3):
                    sp.dma_start(raw[Q * i:Q * (i + 1), s, :].rearrange("q (g v) -> q g v", g=QUADS),
                                 x_dram[i, :, QUADS * s:QUADS * (s + 1), :]).then_inc(first_x_landed[s], DMA)
            with sp.Fori(1, GROUPS) as k:
                for j in range(SLOTS // PAIR):
                    sp.wait_ge(small_ready, SLOTS * (k - 1) + PAIR * (j + 1))
                    for i in (0, 2, 1, 3):
                        sp.dma_start(raw[Q * i:Q * (i + 1), PAIR * j:PAIR * (j + 1), :].rearrange(
                                         "q s (g v) -> q (s g) v", g=QUADS),
                                     x_dram[i, :, bass.ds(QUADS * (SLOTS * k + PAIR * j), QUADS * PAIR), :]
                                     ).then_inc(x_landed[j], DMA)
                for s in range(SLOTS):
                    store(sp, SLOTS * (k - 1) + s, s)
            for s in range(SLOTS):
                store(sp, SLOTS * (GROUPS - 1) + s, s)
            for s in range(SLOTS):
                sp.wait_ge(out_stored[s], DMA * GROUPS)

        @block.gpsimd
        def _(pool):
            for c in range(CHUNKS):
                pool.dma_start(w_raw[:, c, :], w_dram[:, c, :]).then_inc(w_landed[c], DMA)

        @block.scalar
        def _(act):
            def expand_word(s, k):
                nc.scalar.copy(
                    first_mask[:, s, WORD * k:WORD * (k + 1), :],
                    turned[:, s, P * WORD * k:P * WORD * (k + 1)].rearrange("p (b j) -> p j b", j=WORD)
                ).then_inc(mask_ready, 1)

            def expand(tile, into, s):
                act.wait_ge(turned_ready, tile + 1)
                nc.scalar.copy(
                    into[:, s, :, :].rearrange("p (k j) b -> p k j b", j=WORD),
                    turned[:, s, :].rearrange("p (k b j) -> p k j b", k=WORDS, j=WORD)).then_inc(mask_ready, 1)

            def copy_out(tile, s, first):
                act.wait_ge(product_done, tile + 1)
                if not first:
                    act.wait_ge(out_stored[s], DMA * (tile // SLOTS))
                nc.scalar.copy(out_sb[:, s, :], acc[s][:, :]).then_inc(copied, 1)

            for kind, n in ((a[0], int(a[1:])) for a in SCALAR_ORDER):
                if kind == "x":
                    act.wait_ge(turned_ready, n + 1)
                    for k in range(WORDS):
                        expand_word(n, k)
                else:
                    act.wait_ge(w_landed[n], DMA)
                    nc.scalar.copy(w_hi[:, n, :], w_raw[:, n, :]).then_inc(hi_ready, 1)
            expand(SLOTS, mask, 0)
            for k in range(1, GROUPS):
                for s in range(SLOTS):
                    tile = SLOTS * k + s
                    copy_out(tile - SLOTS, s, k == 1)
                    if tile + 1 < TILES:
                        if tile + 1 >= 2 * SLOTS:
                            act.wait_ge(product_done, tile + 1 - SLOTS + 1)
                        expand(tile + 1, mask, (s + 1) % SLOTS)
            for s in range(SLOTS):
                copy_out(SLOTS * (GROUPS - 1) + s, s, False)

        @block.vector
        def _(dve):
            nc.vector.memset(warm[:, :], 0.0).then_inc(warm_ready, 1)

            def turn(tile, s):
                nc.vector.tensor_scalar(small[:, s % 2, :], raw[:, s, :], 0.0, None,
                                        ALU.not_equal).then_inc(small_ready, 1)
                dve.wait_ge(small_ready, tile + 1)
                nc.vector.transpose(
                    turned[:, s, :].bitcast(U32).rearrange("p (k g q) -> p k g q", k=WORDS, g=QUADS),
                    small[:, s % 2, :].bitcast(U32).rearrange("p (g w k) -> p k g w", g=QUADS, k=WORDS)
                ).then_inc(turned_ready, 1)

            for kind, n in ((a[0], int(a[1:])) for a in ORDER):
                if kind == "x":
                    dve.wait_ge(first_x_landed[n], LOAD)
                    turn(n, n)
                else:
                    dve.wait_ge(hi_ready, n + 1)
                    nc.vector.tensor_tensor(w_lo[:, n, :], w_raw[:, n, :], w_hi[:, n, :].bitcast(F32),
                                            ALU.subtract).then_inc(lo_ready, 1)
            with dve.Fori(1, GROUPS) as k:
                for s in range(SLOTS):
                    if s % PAIR == 0:
                        dve.wait_ge(x_landed[s // PAIR], LOAD * k)
                    dve.wait_ge(mask_ready, FIRST_MASKS - SLOTS + SLOTS * (k - 1) + s + 1)
                    turn(SLOTS * k + s, s)

        @block.tensor
        def _(pe):
            pe.wait_ge(warm_ready, 1)
            for n in range(WARM_MATMULS):
                nc.tensor.matmul(warm_acc[:, :], warm[:, 0:P], warm[:, :], start=True, stop=True)

            def unit(s, c, masks, first, last):
                nc.tensor.matmul(acc[s][:, :], masks[:, s, c, :], w_hi[:, c, :], start=first, stop=False)
                return nc.tensor.matmul(acc[s][:, :], masks[:, s, c, :], w_lo[:, c, :], start=False, stop=last)

            tiles, chunks = [], []
            for kind, n in ((a[0], int(a[1:])) for a in ORDER):
                if kind == "x":
                    tiles.append(n)
                    for c in chunks:
                        pe.wait_ge(mask_ready, WORDS * n + c // WORD + 1)
                        last = unit(n, c, first_mask, c == 0, c == CHUNKS - 1)
                else:
                    pe.wait_ge(lo_ready, n + 1)
                    chunks.append(n)
                    for s in tiles:
                        pe.wait_ge(mask_ready, WORDS * s + n // WORD + 1)
                        last = unit(s, n, first_mask, n == 0, n == CHUNKS - 1)
                        if n == CHUNKS - 1:
                            last.then_inc(product_done, 1)
            with pe.Fori(1, GROUPS) as k:
                for s in range(SLOTS):
                    pe.wait_ge(mask_ready, FIRST_MASKS + SLOTS * (k - 1) + s + 1)
                    pe.wait_ge(copied, SLOTS * (k - 1) + s + 1)
                    for c in range(CHUNKS):
                        last = unit(s, c, mask, c == 0, c == CHUNKS - 1)
                    last.then_inc(product_done, 1)


def kernel(r_x, L0_rec_W):
    import numpy as np
    import concourse.bacc as bacc
    from concourse.bass_utils import run_bass_kernel_spmd

    nc = bacc.Bacc("TRN2", target_bir_lowering=False, num_devices=1)
    arrays = {"r_x": np.ascontiguousarray(r_x), "w": np.ascontiguousarray(L0_rec_W)}
    aps = [nc.dram_tensor(name, a.shape, mybir.dt.from_np(a.dtype), kind="ExternalInput").ap()
           for name, a in arrays.items()]
    out = nc.dram_tensor("out", (r_x.shape[0], L0_rec_W.shape[1]), F32, kind="ExternalOutput").ap()
    masked_sum_kernel(nc, *aps, out)
    return run_bass_kernel_spmd(nc, [arrays], core_ids=[0]).results[0]["out"]
```

```python
from contextlib import ExitStack

import concourse.bass as bass
from concourse import mybir

P = 128
Q = 32
QUADS = P // Q
WORD = 4
SLOTS = 4
PAIR = 2
WARM_MATMULS = 12
DMA = 16

ALU = mybir.AluOpType
F32 = mybir.dt.float32
F32R = mybir.dt.float32r
I32 = mybir.dt.int32
U32 = mybir.dt.uint32
U8 = mybir.dt.uint8
BF16 = mybir.dt.bfloat16

FIRST_LOADS = [(0, 0, 2), (0, 2, 2), (1, 0, 2), (1, 2, 2)]
SCALAR_ORDER = "w0 w1 x00 x10 w2 w3 x20 x30 w4 w5 x01 x11 w6 w7 x21 x31".split()
VECTOR_ORDER = "x00 x10 w0 w1 w2 x20 x30 w3 x01 w4 x11 w5 x21 x31 w6 w7".split()
TENSOR_ORDER = ("h0 x00 h1 l0 x10 l1 h2 l2 h3 x20 l3 "
                "x30 h4 x01 l4 h5 x11 l5 h6 l6 h7 x21 l7 x31").split()


def half_tiles(order):
    return [tuple(map(int, a[1:])) for a in order if a[0] == "x"]


assert half_tiles(SCALAR_ORDER) == half_tiles(VECTOR_ORDER) == half_tiles(TENSOR_ORDER)


def masked_sum_kernel(nc: bass.Bass, r_x: bass.AP, w: bass.AP, out: bass.AP):
    B, V = r_x.shape
    D = w.shape[1]
    CHUNKS = V // P
    HALVES = CHUNKS // WORD
    TILES = B // P
    GROUPS = TILES // SLOTS
    FIRST = SLOTS * HALVES
    RUN = WORD * Q
    assert V == P * WORD * HALVES and B == P * SLOTS * GROUPS and D * 4 == 2048
    assert sorted(half_tiles(TENSOR_ORDER)) == [(s, h) for s in range(SLOTS) for h in range(HALVES)]

    x_dram = r_x.rearrange("(tg q) (h i v) -> h i q tg v", q=Q, h=HALVES, i=QUADS)
    w_dram = w.rearrange("(h p j) d -> h p j d", h=HALVES, j=WORD)
    out_dram = out.rearrange("(t p) d -> t p d", p=P)

    with ExitStack() as ctx:
        def sb(name, shape, dt):
            return ctx.enter_context(nc.sbuf_tensor(name, shape, dt))

        def bank(name):
            return ctx.enter_context(nc.psum_tensor(name, [P, D], F32))

        def sem(name):
            return ctx.enter_context(nc.semaphore(name))

        w_raw = sb("w_raw", [P, CHUNKS, D], F32)
        w_hi = sb("w_hi", [P, CHUNKS, D], F32R)
        w_lo = sb("w_lo", [P, CHUNKS, D], F32R)
        first_raw = sb("first_raw", [P, HALVES, SLOTS, QUADS * RUN], I32)
        raw = sb("raw", [P, HALVES, SLOTS, QUADS * RUN], I32)
        small = sb("small", [P, 2, HALVES, QUADS * RUN], U8)
        turned = sb("turned", [P, SLOTS, HALVES, P * WORD], U8)
        first_mask = sb("first_mask", [P, SLOTS, CHUNKS, P], F32R)
        mask = sb("mask", [P, SLOTS, CHUNKS, P], F32R)
        out_sb = sb("out_sb", [P, TILES, D], F32)
        warm = sb("warm", [P, D], BF16)
        acc = [bank(f"acc{s}") for s in range(SLOTS)]
        side_acc = bank("side_acc")

        first_x_landed = [sem(f"first_x_landed{n}") for n in range(len(FIRST_LOADS))]
        x_landed = [sem(f"x_landed{j}") for j in range(SLOTS // PAIR)]
        w_landed = [sem(f"w_landed{c}") for c in range(CHUNKS)]
        out_stored = sem("out_stored")
        last_stored = sem("last_stored")
        warm_ready = sem("warm_ready")
        hi_ready = sem("hi_ready")
        lo_ready = sem("lo_ready")
        small_ready = sem("small_ready")
        turned_ready = sem("turned_ready")
        mask_ready = sem("mask_ready")
        product_done = sem("product_done")
        copied = sem("copied")

        load_of = {(s, h): n for n, (h, s0, count) in enumerate(FIRST_LOADS) for s in range(s0, s0 + count)}
        LEFT, RIGHT = slice(0, D // 2), slice(D // 2, D)

        def tokens(order):
            return [(a[0], tuple(map(int, a[1:]))) for a in order]

        block = ctx.enter_context(nc.Block())

        @block.sync
        def _(sp):
            def load(into, h, tile, slot, count, landed):
                for i in (0, 2, 1, 3):
                    sp.dma_start(
                        into[Q * i:Q * (i + 1), h, slot:slot + count, :].rearrange(
                            "q s (g v) -> q (s g) v", g=QUADS),
                        x_dram[h, i, :, bass.ds(QUADS * tile, QUADS * count), :]).then_inc(landed, DMA)

            for n, (h, s, count) in enumerate(FIRST_LOADS):
                load(first_raw, h, s, s, count, first_x_landed[n])

            def load_pair(k, j):
                for h in range(HALVES):
                    load(raw, h, SLOTS * k + PAIR * j, PAIR * j, PAIR, x_landed[j])

            for j in range(SLOTS // PAIR):
                load_pair(1, j)
            with sp.Fori(2, GROUPS) as k:
                for j in range(SLOTS // PAIR):
                    sp.wait_ge(small_ready, FIRST + SLOTS * (k - 2) + PAIR * (j + 1))
                    load_pair(k, j)
            for n, columns in enumerate((LEFT, RIGHT)):
                sp.wait_ge(copied, TILES + n)
                sp.dma_start(out_dram[TILES - 1][:, columns],
                             out_sb[:, TILES - 1, columns]).then_inc(last_stored, DMA)
            sp.wait_ge(out_stored, DMA * (TILES - 1))
            sp.wait_ge(last_stored, DMA * 2)

        @block.gpsimd
        def _(pool):
            for c in range(CHUNKS):
                pool.dma_start(w_raw[:, c, :], w_dram[c // WORD, :, c % WORD, :]).then_inc(w_landed[c], DMA)

            def store(tile):
                pool.wait_ge(copied, tile + 1)
                pool.dma_start(out_dram[tile], out_sb[:, tile, :]).then_inc(out_stored, DMA)

            with pool.Fori(0, GROUPS - 1) as k:
                for s in range(SLOTS):
                    store(SLOTS * k + s)
            for tile in range(TILES - SLOTS, TILES - 1):
                store(tile)

        @block.scalar
        def _(act):
            def expand(tile, s):
                act.wait_ge(turned_ready, FIRST + tile - SLOTS + 1)
                nc.scalar.copy(mask[:, s, :, :].rearrange("p (h j) b -> p h j b", j=WORD),
                               turned[:, s, :, :].rearrange("p h (b j) -> p h j b", j=WORD)
                               ).then_inc(mask_ready, 1)

            def copy_out(tile, s):
                act.wait_ge(product_done, tile + 1)
                nc.scalar.copy(out_sb[:, tile, :], acc[s][:, :]).then_inc(copied, 1)

            step = 0
            for kind, at in tokens(SCALAR_ORDER):
                if kind == "w":
                    c, = at
                    act.wait_ge(w_landed[c], DMA)
                    nc.scalar.copy(w_hi[:, c, :], w_raw[:, c, :]).then_inc(hi_ready, 1)
                else:
                    s, h = at
                    step += 1
                    act.wait_ge(turned_ready, step)
                    nc.scalar.copy(first_mask[:, s, WORD * h:WORD * (h + 1), :],
                                   turned[:, s, h, :].rearrange("p (b j) -> p j b", j=WORD)
                                   ).then_inc(mask_ready, 1)
            expand(SLOTS, 0)

            def group(k, slots):
                for s in slots:
                    copy_out(SLOTS * (k - 1) + s, s)
                    act.wait_ge(product_done, SLOTS * (k - 1) + s + 2)
                    expand(SLOTS * k + s + 1, (s + 1) % SLOTS)

            with act.Fori(1, GROUPS - 1) as k:
                group(k, range(SLOTS))
            group(GROUPS - 1, range(SLOTS - 1))
            for tile in range(TILES - SLOTS - 1, TILES - 1):
                copy_out(tile, tile % SLOTS)
            act.wait_ge(product_done, TILES)
            nc.scalar.copy(out_sb[:, TILES - 1, LEFT], side_acc[:, LEFT]).then_inc(copied, 1)
            act.wait_ge(product_done, TILES + 1)
            nc.scalar.copy(out_sb[:, TILES - 1, RIGHT], acc[SLOTS - 1][:, RIGHT]).then_inc(copied, 1)

        @block.vector
        def _(dve):
            nc.vector.memset(warm[:, :], 0.0).then_inc(warm_ready, 1)

            def turn(tiles, s, halves, step, buffer, reused):
                if reused:
                    dve.wait_ge(turned_ready, step - 2)
                nc.vector.tensor_scalar(small[:, buffer, halves, :], tiles[:, halves, s, :], 0.0, None,
                                        ALU.not_equal).then_inc(small_ready, 1)
                dve.wait_ge(small_ready, step)
                nc.vector.transpose(turned[:, s, halves, :].bitcast(U32),
                                    small[:, buffer, halves, :].bitcast(U32)).then_inc(turned_ready, 1)

            step = 0
            for kind, at in tokens(VECTOR_ORDER):
                if kind == "w":
                    c, = at
                    dve.wait_ge(hi_ready, c + 1)
                    nc.vector.tensor_tensor(w_lo[:, c, :], w_raw[:, c, :], w_hi[:, c, :].bitcast(F32),
                                            ALU.subtract).then_inc(lo_ready, 1)
                else:
                    s, h = at
                    step += 1
                    dve.wait_ge(first_x_landed[load_of[s, h]], QUADS * DMA)
                    turn(first_raw, s, slice(h, h + 1), step, step % 2, step > 2)
            with dve.Fori(1, GROUPS) as k:
                for s in range(SLOTS):
                    if s % PAIR == 0:
                        dve.wait_ge(x_landed[s // PAIR], HALVES * QUADS * DMA * k)
                    dve.wait_ge(mask_ready, FIRST + SLOTS * (k - 2) + s + 1)
                    turn(raw, s, slice(0, HALVES), FIRST + SLOTS * (k - 1) + s + 1, (s + 1) % 2, True)

        @block.tensor
        def _(pe):
            pe.wait_ge(warm_ready, 1)
            for n in range(WARM_MATMULS):
                nc.tensor.matmul(side_acc[:, :], warm[:, 0:P], warm[:, :], start=True, stop=True)

            def chunk(into, masks, s, c, columns=slice(0, D)):
                nc.tensor.matmul(into[:, columns], masks[:, s, c, :], w_hi[:, c, columns],
                                 start=c == 0, stop=False)
                return nc.tensor.matmul(into[:, columns], masks[:, s, c, :], w_lo[:, c, columns],
                                        start=False, stop=c == CHUNKS - 1)

            masks, parts, products = [], [], [0] * SLOTS
            for kind, at in tokens(TENSOR_ORDER):
                if kind == "x":
                    masks.append(at)
                    pe.wait_ge(mask_ready, len(masks))
                    pairs = [(at[0], part, c) for part, c in parts if c // WORD == at[1]]
                else:
                    c, = at
                    part = w_hi if kind == "h" else w_lo
                    parts.append((part, c))
                    pe.wait_ge(hi_ready if kind == "h" else lo_ready, c + 1)
                    pairs = [(s, part, c) for s, h in masks if h == c // WORD]
                for s, part, c in pairs:
                    products[s] += 1
                    last = nc.tensor.matmul(acc[s][:, :], first_mask[:, s, c, :], part[:, c, :],
                                            start=products[s] == 1, stop=products[s] == 2 * CHUNKS)
                    if products[s] == 2 * CHUNKS:
                        assert products[s + 1:] == [n for n in products[s + 1:] if n < 2 * CHUNKS]
                        last.then_inc(product_done, 1)

            def whole_tile(k, s):
                pe.wait_ge(mask_ready, FIRST + SLOTS * (k - 1) + s + 1)
                pe.wait_ge(copied, SLOTS * (k - 1) + s + 1)
                for c in range(CHUNKS):
                    last = chunk(acc[s], mask, s, c)
                last.then_inc(product_done, 1)

            with pe.Fori(1, GROUPS - 1) as k:
                for s in range(SLOTS):
                    whole_tile(k, s)
            for s in range(SLOTS - 1):
                whole_tile(GROUPS - 1, s)
            s = SLOTS - 1
            pe.wait_ge(mask_ready, FIRST + TILES - SLOTS)
            for into, columns in ((side_acc, LEFT), (acc[s], RIGHT)):
                if columns == RIGHT:
                    pe.wait_ge(copied, TILES - SLOTS)
                for c in range(CHUNKS):
                    last = chunk(into, mask, s, c, columns)
                last.then_inc(product_done, 1)


def kernel(r_x, L0_rec_W):
    import numpy as np
    import concourse.bacc as bacc
    from concourse.bass_utils import run_bass_kernel_spmd

    nc = bacc.Bacc("TRN2", target_bir_lowering=False, num_devices=1)
    arrays = {"r_x": np.ascontiguousarray(r_x), "w": np.ascontiguousarray(L0_rec_W)}
    aps = [nc.dram_tensor(name, a.shape, mybir.dt.from_np(a.dtype), kind="ExternalInput").ap()
           for name, a in arrays.items()]
    out = nc.dram_tensor("out", (r_x.shape[0], L0_rec_W.shape[1]), F32, kind="ExternalOutput").ap()
    masked_sum_kernel(nc, *aps, out)
    return run_bass_kernel_spmd(nc, [arrays], core_ids=[0]).results[0]["out"]
```
